# Optimizing a Trainium2 kernel written in Bass

```python
import numpy as np
import jax
import jax.numpy as jnp

def _softmax(x, axis=-1):
    return jax.nn.softmax(x, axis=axis)

def _gelu(x):
    return jax.nn.gelu(x, approximate=True)

def _silu(x):
    return jax.nn.silu(x)

def _sigmoid(x):
    return jax.nn.sigmoid(x)

def _layernorm(x, axis=-1, eps=1e-05):
    m = jnp.mean(x, axis=axis, keepdims=True)
    v = jnp.var(x, axis=axis, keepdims=True)
    return (x - m) / jnp.sqrt(v + eps)

def _scatter_add(tgt, idx, src, axis=0):
    return tgt.at[idx].add(src)

def _segment_sum(src, seg, n):
    return jax.ops.segment_sum(src, seg, n)
kernel_name = 'mk_dlrm_tower_d1_rec_r8_455df3'

def setup_inputs(seed: int=0):
    np.random.seed(seed)
    _w = jnp.asarray

    def _rec_inputs():
        import jax
        import jax.numpy as jnp
        _tk = jax.random.key(seed)
        dense_ctx = jax.random.normal(jax.random.fold_in(_tk, 190), (2048, 16), jnp.float32)
        ids = jnp.stack([jax.random.randint(jax.random.fold_in(_tk, 200 + f), (2048,), 0, v, jnp.int32) for f, v in enumerate([1000, 1250, 125000, 1250, 1250, 1000, 12500, 12500, 1000, 1250, 1250, 12500, 1000, 1250, 1000, 1000, 1250, 1000, 1250, 12500, 1250, 1000, 12500, 12500, 12500, 12500, 1250])], axis=1)
        tbl_0 = 0.05 * jax.random.normal(jax.random.fold_in(_tk, 500 + 0), (1000, 128), jnp.float32)
        tbl_1 = 0.05 * jax.random.normal(jax.random.fold_in(_tk, 500 + 1), (1250, 128), jnp.float32)
        tbl_2 = 0.05 * jax.random.normal(jax.random.fold_in(_tk, 500 + 2), (125000, 128), jnp.float32)
        tbl_3 = 0.05 * jax.random.normal(jax.random.fold_in(_tk, 500 + 3), (1250, 128), jnp.float32)
        tbl_4 = 0.05 * jax.random.normal(jax.random.fold_in(_tk, 500 + 4), (1250, 128), jnp.float32)
        tbl_5 = 0.05 * jax.random.normal(jax.random.fold_in(_tk, 500 + 5), (1000, 128), jnp.float32)
        tbl_6 = 0.05 * jax.random.normal(jax.random.fold_in(_tk, 500 + 6), (12500, 128), jnp.float32)
        tbl_7 = 0.05 * jax.random.normal(jax.random.fold_in(_tk, 500 + 7), (12500, 128), jnp.float32)
        tbl_8 = 0.05 * jax.random.normal(jax.random.fold_in(_tk, 500 + 8), (1000, 128), jnp.float32)
        tbl_9 = 0.05 * jax.random.normal(jax.random.fold_in(_tk, 500 + 9), (1250, 128), jnp.float32)
        tbl_10 = 0.05 * jax.random.normal(jax.random.fold_in(_tk, 500 + 10), (1250, 128), jnp.float32)
        tbl_11 = 0.05 * jax.random.normal(jax.random.fold_in(_tk, 500 + 11), (12500, 128), jnp.float32)
        tbl_12 = 0.05 * jax.random.normal(jax.random.fold_in(_tk, 500 + 12), (1000, 128), jnp.float32)
        tbl_13 = 0.05 * jax.random.normal(jax.random.fold_in(_tk, 500 + 13), (1250, 128), jnp.float32)
        tbl_14 = 0.05 * jax.random.normal(jax.random.fold_in(_tk, 500 + 14), (1000, 128), jnp.float32)
        tbl_15 = 0.05 * jax.random.normal(jax.random.fold_in(_tk, 500 + 15), (1000, 128), jnp.float32)
        tbl_16 = 0.05 * jax.random.normal(jax.random.fold_in(_tk, 500 + 16), (1250, 128), jnp.float32)
        tbl_17 = 0.05 * jax.random.normal(jax.random.fold_in(_tk, 500 + 17), (1000, 128), jnp.float32)
        tbl_18 = 0.05 * jax.random.normal(jax.random.fold_in(_tk, 500 + 18), (1250, 128), jnp.float32)
        tbl_19 = 0.05 * jax.random.normal(jax.random.fold_in(_tk, 500 + 19), (12500, 128), jnp.float32)
        tbl_20 = 0.05 * jax.random.normal(jax.random.fold_in(_tk, 500 + 20), (1250, 128), jnp.float32)
        tbl_21 = 0.05 * jax.random.normal(jax.random.fold_in(_tk, 500 + 21), (1000, 128), jnp.float32)
        tbl_22 = 0.05 * jax.random.normal(jax.random.fold_in(_tk, 500 + 22), (12500, 128), jnp.float32)
        tbl_23 = 0.05 * jax.random.normal(jax.random.fold_in(_tk, 500 + 23), (12500, 128), jnp.float32)
        tbl_24 = 0.05 * jax.random.normal(jax.random.fold_in(_tk, 500 + 24), (12500, 128), jnp.float32)
        tbl_25 = 0.05 * jax.random.normal(jax.random.fold_in(_tk, 500 + 25), (12500, 128), jnp.float32)
        tbl_26 = 0.05 * jax.random.normal(jax.random.fold_in(_tk, 500 + 26), (1250, 128), jnp.float32)
        _rk = jax.random.fold_in(_tk, 7)
        W_top1 = 0.0521996 * jax.random.normal(jax.random.fold_in(_tk, 801), (367, 512), jnp.float32)
        W_top2 = 0.0441942 * jax.random.normal(jax.random.fold_in(_tk, 802), (512, 256), jnp.float32)
        W_top3 = 0.0625 * jax.random.normal(jax.random.fold_in(_tk, 803), (256, 1), jnp.float32)
        b_top1 = jnp.zeros((512,), jnp.float32)
        b_top2 = jnp.zeros((256,), jnp.float32)
        return (dense_ctx, ids, tbl_0, tbl_1, tbl_2, tbl_3, tbl_4, tbl_5, tbl_6, tbl_7, tbl_8, tbl_9, tbl_10, tbl_11, tbl_12, tbl_13, tbl_14, tbl_15, tbl_16, tbl_17, tbl_18, tbl_19, tbl_20, tbl_21, tbl_22, tbl_23, tbl_24, tbl_25, tbl_26, W_top1, b_top1, W_top2, b_top2, W_top3)
    dense_ctx, ids, tbl_0, tbl_1, tbl_2, tbl_3, tbl_4, tbl_5, tbl_6, tbl_7, tbl_8, tbl_9, tbl_10, tbl_11, tbl_12, tbl_13, tbl_14, tbl_15, tbl_16, tbl_17, tbl_18, tbl_19, tbl_20, tbl_21, tbl_22, tbl_23, tbl_24, tbl_25, tbl_26, W_top1, b_top1, W_top2, b_top2, W_top3 = _rec_inputs()

    def _L0_rec_setup():
        import jax, jax.numpy as jnp
        import numpy as np

        def _tri_indices(num_feas):
            return np.array([i * num_feas + j for j in range(1, num_feas) for i in range(j)], dtype=np.int32)
        key = jax.random.key(seed)
        batch, num_feas, embed_dim = (2048, 27, 128)
        inputs = jax.random.normal(key, (batch, num_feas, embed_dim), dtype=jnp.float32)
        return {'inputs': inputs, 'num_feas': num_feas}
    _L0_rec_all = _L0_rec_setup()
    _L0_rec_in = {k: v for k, v in _L0_rec_all.items() if k in ()}
    del _L0_rec_all
    return {'dense_ctx': dense_ctx, 'ids': ids, 'tbl_0': tbl_0, 'tbl_1': tbl_1, 'tbl_2': tbl_2, 'tbl_3': tbl_3, 'tbl_4': tbl_4, 'tbl_5': tbl_5, 'tbl_6': tbl_6, 'tbl_7': tbl_7, 'tbl_8': tbl_8, 'tbl_9': tbl_9, 'tbl_10': tbl_10, 'tbl_11': tbl_11, 'tbl_12': tbl_12, 'tbl_13': tbl_13, 'tbl_14': tbl_14, 'tbl_15': tbl_15, 'tbl_16': tbl_16, 'tbl_17': tbl_17, 'tbl_18': tbl_18, 'tbl_19': tbl_19, 'tbl_20': tbl_20, 'tbl_21': tbl_21, 'tbl_22': tbl_22, 'tbl_23': tbl_23, 'tbl_24': tbl_24, 'tbl_25': tbl_25, 'tbl_26': tbl_26, 'W_top1': W_top1, 'b_top1': b_top1, 'W_top2': W_top2, 'b_top2': b_top2, 'W_top3': W_top3}

def reference(dense_ctx, ids, tbl_0, tbl_1, tbl_2, tbl_3, tbl_4, tbl_5, tbl_6, tbl_7, tbl_8, tbl_9, tbl_10, tbl_11, tbl_12, tbl_13, tbl_14, tbl_15, tbl_16, tbl_17, tbl_18, tbl_19, tbl_20, tbl_21, tbl_22, tbl_23, tbl_24, tbl_25, tbl_26, W_top1, b_top1, W_top2, b_top2, W_top3):
    import jax
    import jax.numpy as jnp

    def _L0_rec_ref(inputs, num_feas):
        import jax, jax.numpy as jnp
        import numpy as np

        def _tri_indices(num_feas):
            return np.array([i * num_feas + j for j in range(1, num_feas) for i in range(j)], dtype=np.int32)
        dot = jnp.einsum('bnd,bmd->bnm', inputs, inputs)
        idx = jnp.asarray(_tri_indices(num_feas))
        flat = dot.reshape(inputs.shape[0], num_feas * num_feas)
        return flat[:, idx]
    e = jnp.stack([tbl_0[ids[:, 0]], tbl_1[ids[:, 1]], tbl_2[ids[:, 2]], tbl_3[ids[:, 3]], tbl_4[ids[:, 4]], tbl_5[ids[:, 5]], tbl_6[ids[:, 6]], tbl_7[ids[:, 7]], tbl_8[ids[:, 8]], tbl_9[ids[:, 9]], tbl_10[ids[:, 10]], tbl_11[ids[:, 11]], tbl_12[ids[:, 12]], tbl_13[ids[:, 13]], tbl_14[ids[:, 14]], tbl_15[ids[:, 15]], tbl_16[ids[:, 16]], tbl_17[ids[:, 17]], tbl_18[ids[:, 18]], tbl_19[ids[:, 19]], tbl_20[ids[:, 20]], tbl_21[ids[:, 21]], tbl_22[ids[:, 22]], tbl_23[ids[:, 23]], tbl_24[ids[:, 24]], tbl_25[ids[:, 25]], tbl_26[ids[:, 26]]], axis=1)
    z = _L0_rec_ref(e, 27)
    z = z.reshape(z.shape[0], -1)
    h = jnp.concatenate([z, dense_ctx], axis=1)
    h = jnp.maximum(h @ W_top1 + b_top1, 0.0)
    h = jnp.maximum(h @ W_top2 + b_top2, 0.0)
    y = h @ W_top3
    return y

_drawn_inputs = setup_inputs


def setup_inputs(seed=0):
    import zlib

    import numpy as np

    out = dict(_drawn_inputs(seed))
    spreads = {'b_top1': (0.0, 0.1), 'b_top2': (0.0, 0.1)}
    factors = {}
    for name, (base, spread) in spreads.items():
        noise = np.random.default_rng([zlib.crc32(name.encode()), seed]).standard_normal(out[name].shape)
        drawn = base * np.exp(spread * noise) if base else spread * noise
        out[name] = jnp.asarray(drawn.astype(out[name].dtype))
    for name, factor in factors.items():
        out[name] = (out[name] * factor).astype(out[name].dtype)
    return out
```

```python
import concourse.bass as bass
from concourse import mybir
from contextlib import ExitStack

P = 128
BATCH = 2048
NF = 27
ST = 4
NS = BATCH // (ST * P)
TABLE_ROWS = [1000, 1250, 125000, 1250, 1250, 1000, 12500, 12500, 1000, 1250, 1250, 12500, 1000, 1250, 1000, 1000,
              1250, 1000, 1250, 12500, 1250, 1000, 12500, 12500, 12500, 12500, 1250]
HOT_ROWS = 1000
HOT = [f for f in range(NF) if TABLE_ROWS[f] == HOT_ROWS]
COLD = [f for f in range(NF) if TABLE_ROWS[f] != HOT_ROWS]
SLOTS = COLD + HOT
NH, NC = len(HOT), len(COLD)
CR = 125
CH = HOT_ROWS // CR
NDIST = (NF - 1) // 2
JC = 9
KC = NF // JC
KP = JC * NDIST
ND = 16
D0 = P - KP
D1 = ND - D0
KROWS = [P, KP + D1 + 1, KP]
H1, H2 = 512, 256
M1, M2 = H1 // P, H2 // P
SG = 32
HG = SG // 2
IW = NF + NDIST
TG = 4
NG = -(-NC // TG)


def pair_rows():
    rows = []
    for j in range(NF):
        for d in range(1, NDIST + 1):
            a, b = SLOTS[j], SLOTS[(j + d) % NF]
            hi, lo = max(a, b), min(a, b)
            rows.append(hi * (hi - 1) // 2 + lo)
    return rows


def dlrm_tower(nc, x):
    fp32, f32r, i32 = mybir.dt.float32, mybir.dt.float32r, mybir.dt.int32
    ALU = mybir.AluOpType
    ACT = mybir.ActivationFunctionType

    with ExitStack() as ctx:
        def sb(name, shape, dt=fp32):
            return ctx.enter_context(nc.sbuf_tensor(name, shape, dt))

        def ps(name, shape):
            return ctx.enter_context(nc.psum_tensor(name, shape, fp32))

        def sem(name):
            return ctx.enter_context(nc.semaphore(name))

        eT = sb("eT", [P, ST, P, NF])
        table_hi = sb("table_hi", [CR, NH, CH, P], f32r)
        table_lo = sb("table_lo", [CR, NH, CH, P], f32r)
        rows = [sb(f"rows{i}", [P, NC, P]) for i in range(2)]
        hot_ids = sb("hot_ids", [P, NH, ST * P], i32)
        onehot = sb("onehot", [CR, CH, ST * P], f32r)
        row_number = sb("row_number", [P, CH])
        cold_ids = sb("cold_ids", [P, ST, NC], i32)
        ident = sb("ident", [P, P])
        dots = [sb(f"dots{i}", [P, IW, SG]) for i in range(2)]
        zT = [sb(f"zT{i}", [P, KC, P]) for i in range(2)]
        w1 = sb("w1", [P, KC, H1])
        w2 = sb("w2", [P, M1, H2])
        w3 = sb("w3", [P, M2])
        b2 = sb("b2", [P, M2])
        h1 = sb("h1", [P, M1, P])
        h2 = sb("h2", [P, M2, P])
        y = [sb(f"y{i}", [1, P]) for i in range(2)]
        raw_tables = eT[:, :, :, :].rearrange("p t s f -> p (t s f)")[0:CR, 0:NH * CH * P]\
            .rearrange("p (k c d) -> p k c d", k=NH, c=CH)

        scratch = [nc.dram_tensor(f"dots_scratch{i}", (SG, IW, P), fp32, kind="Internal").ap() for i in range(2)]

        ps_hot = [ps(f"ps_hot{i}", [P, ST * P]) for i in range(2)]
        ps_tr = [ps(f"ps_tr{i}", [P, TG, P]) for i in range(2)]
        ps_dot = [ps(f"ps_dot{i}", [P, HG, 32]) for i in range(2)]
        ps_h1 = ps("ps_h1", [P, M1, P])
        ps_h2 = ps("ps_h2", [P, 4, P])

        cold_ids_ready = [sem(f"cold_ids_ready{i}") for i in range(ST)]
        hot_ids_ready = sem("hot_ids_ready")
        raw_ready = [sem(f"raw_ready{h}") for h in range(NH)]
        w1_ready = sem("w1_ready")
        w23_ready = sem("w23_ready")
        b2_ready = sem("b2_ready")
        dense_ready = [sem(f"dense_ready{i}") for i in range(2)]
        row_number_ready = sem("row_number_ready")
        ident_zero = sem("ident_zero")
        ident_ready = sem("ident_ready")
        cleared = sem("cleared")
        hi_ready = sem("hi_ready")
        lo_ready = sem("lo_ready")
        onehot_ready = sem("onehot_ready")
        onehot_used = [sem(f"onehot_used{i}") for i in range(CH)]
        hot_read = [sem(f"hot_read{i}") for i in range(2)]
        rows_ready = [sem(f"rows_ready{i}") for i in range(2)]
        transposed = [sem(f"transposed{i}") for i in range(2)]
        tr_read = [sem(f"tr_read{i}") for i in range(2)]
        dot_done = [sem(f"dot_done{i}") for i in range(2)]
        dot_read = [sem(f"dot_read{i}") for i in range(2)]
        dots_stored = [sem(f"dots_stored{i}") for i in range(2)]
        z_ready = [sem(f"z_ready{i}") for i in range(2)]
        l1_done = sem("l1_done")
        h1_ready = sem("h1_ready")
        l2_done = sem("l2_done")
        h2_ready = sem("h2_ready")
        l3_done = sem("l3_done")
        y_ready = sem("y_ready")
        y_stored = [sem(f"y_stored{i}") for i in range(2)]

        sync_waited = sem("sync_waited")
        pool_waited = sem("pool_waited")

        block = ctx.enter_context(nc.Block())

        def tile(n, t):
            return ST * n + t

        def uses(n, t):
            return (ST // 2) * n + t // 2

        def tr_pair(t, g):
            return (NG * t + g) % 2

        def bank_uses(n, t, g):
            return (NG * ST // 2) * n + (NG * t + g) // 2

        def banks_through(n, t, pair):
            return (NG * ST // 2) * n + (NG * (t + 1) + 1 - pair) // 2

        def hot_uses(n, h):
            return (NH // 2) * n + h // 2

        def before(n, t):
            return (n, t - 1) if t else (n - 1, ST - 1)

        def group(g):
            return range(TG * g, min(TG * g + TG, NC))

        @block.sync
        def _(sp):
            def wait(signal, count):
                sp.wait_ge(signal, count)
                sp.sem_inc(sync_waited, 1)

            def load_cold_ids(n, t):
                sp.dma_start(cold_ids[:, t, :], x["cold_ids"][bass.ds(tile(n, t) * P, P), :])\
                  .then_inc(cold_ids_ready[t], 16)

            def load_hot_ids(n):
                sp.dma_start(hot_ids[:, :, :], x["hot_ids"][:, bass.ds(n * (ST * P), ST * P)].partition_broadcast(P))\
                  .then_inc(hot_ids_ready, 16)

            def store_y(n, t):
                wait(y_ready, tile(n, t) + 1)
                sp.dma_start(x["y"][bass.ds(tile(n, t) * P, P), :].rearrange("s o -> o s"), y[t % 2][0:1, :])\
                  .then_inc(y_stored[t % 2], 16)

            def supertile(n, first):
                for t in range(ST):
                    i = t % 2
                    samples = bass.ds(tile(n, t) * P, P)
                    if not (first and t == 0):
                        wait(l1_done, tile(n, t) - 1)
                    sp.dma_start(zT[i][KP:P, 0, :], x["dense"][0:D0, samples]).then_inc(dense_ready[i], 16)
                    sp.dma_start(zT[i][KP:KP + D1, 1, :], x["dense"][D0:ND, samples]).then_inc(dense_ready[i], 16)
                    if t == 1:
                        wait(onehot_ready, NH * CH * (n + 1))
                        load_hot_ids(n + 1)
                    wait(rows_ready[i], NC * 16 * (uses(n, t) + 1))
                    load_cold_ids(n + 1, t)
                    wait(z_ready[i], 16 * KC * uses(n, t))
                    wait(dot_read[0], tile(n, t) + 1)
                    wait(dot_read[1], tile(n, t) + 1)
                    for s in range(4):
                        sp.dma_start(scratch[i][:, :, SG * s:SG * s + SG], dots[i][SG * s:SG * s + SG, :, :])\
                          .then_inc(dots_stored[i], 16)
                    wait(dots_stored[i], 64 * (uses(n, t) + 1))
                    for c in range(KC):
                        pairs = bass.AP(scratch[i].tensor, (JC * c * IW + JC * c + 1) * P,
                                        [[(IW + 1) * P, JC], [P, NDIST], [1, P]])
                        sp.dma_start(zT[i][0:KP, c, :], pairs).then_inc(z_ready[i], 16)
                    if not (first and t == 0):
                        store_y(*before(n, t))

            for t in range(ST):
                load_cold_ids(0, t)
            load_hot_ids(0)
            for h in range(0, NH, 2):
                sp.dma_start(raw_tables[:, h], x["hot"][h].rearrange("(c p) d -> p c d", p=CR))\
                  .then_inc(raw_ready[h], 16)
            sp.wait_ge(cleared, 4)
            supertile(0, True)
            with sp.Fori(1, NS) as n:
                supertile(n, False)
            store_y(NS - 1, ST - 1)
            for i in range(2):
                sp.wait_ge(y_stored[i], 16 * (ST // 2) * NS)
                sp.wait_ge(dots_stored[i], 64 * (ST // 2) * NS)
            for t in range(ST):
                sp.wait_ge(cold_ids_ready[t], 16 * (NS + 1))
            sp.wait_ge(hot_ids_ready, 16 * (NS + 1))

        @block.gpsimd
        def _(pool):
            def supertile(n):
                for t in range(ST):
                    i = t % 2
                    pool.wait_ge(cold_ids_ready[t], 16 * (n + 1))
                    pool.wait_ge(transposed[i], NG * uses(n, t))
                    pool.sem_inc(pool_waited, 1)
                    for f in range(NC):
                        pool.indirect_dma_start(
                            out=rows[i][:, f, :], out_offset=None, in_=x["cold"][f][:, :],
                            in_offset=bass.IndirectOffsetOnAxis(ap=cold_ids[:, t, f:f + 1], axis=0),
                        ).then_inc(rows_ready[i], 16)

            pool.iota(row_number[:, :], pattern=[[CR, CH]], base=0, channel_multiplier=1,
                      allow_small_or_imprecise_dtypes=True).then_inc(row_number_ready, 1)
            pool.memset(ident[:, :], 0.0).then_inc(ident_zero, 1)
            pool.wait_ge(ident_zero, 1)
            pool.affine_select(out=ident[:, :], in_=ident[:, :], compare_op=ALU.not_equal, fill=1.0, base=0,
                               pattern=[[-1, P]], channel_multiplier=1).then_inc(ident_ready, 1)
            supertile(0)
            with pool.Fori(1, NS) as n:
                supertile(n)

        @block.vector
        def _(dve):
            def supertile(n, first):
                dve.wait_ge(hot_ids_ready, 16 * (n + 1))
                for h in range(NH):
                    for c in range(CH):
                        dve.wait_ge(onehot_used[c], NH * n + h)
                        dve.tensor_scalar(onehot[:, c, :], hot_ids[0:CR, h, :], row_number[0:CR, c:c + 1], None,
                                          ALU.is_equal).then_inc(onehot_ready, 1)
                for t in range(ST):
                    i = t % 2
                    for g in range(NG):
                        if tr_pair(t, g) == 1:
                            f = group(g)
                            dve.wait_ge(transposed[i], NG * uses(n, t) + g + 1)
                            dve.wait_ge(dot_done[0], tile(n, t) - t)
                            dve.wait_ge(dot_done[1], tile(n, t) - t)
                            dve.tensor_copy(eT[:, t, :, f[0]:f[-1] + 1],
                                            ps_tr[1][:, 0:len(f), :].rearrange("d f s -> d s f"))\
                               .then_inc(tr_read[1], 1)
                    dve.wait_ge(dot_done[0], tile(n, t) + 1)
                    dve.wait_ge(dots_stored[i], 64 * uses(n, t))
                    dve.tensor_copy(dots[i][:, 0:NF, 0:HG], ps_dot[0][:, :, 0:NF].rearrange("p g i -> p i g"))
                    dve.tensor_copy(dots[i][:, NF:IW, 0:HG], ps_dot[0][:, :, 0:NDIST].rearrange("p g i -> p i g"))\
                       .then_inc(dot_read[0], 1)

            for i in range(2):
                dve.memset(zT[i][96:P, 1, :], 1.0).then_inc(cleared, 1)
            for q in range(2):
                dve.memset(ps_dot[q][:, :, :], 0.0).then_inc(cleared, 1)
            for h in range(NH):
                dve.wait_ge(hi_ready, h + 1)
                dve.tensor_tensor(table_lo[:, h], raw_tables[:, h], table_hi[:, h], ALU.subtract).then_inc(lo_ready, 1)
            dve.wait_ge(row_number_ready, 1)
            supertile(0, True)
            with dve.Fori(1, NS) as n:
                supertile(n, False)

        @block.scalar
        def _(act):
            def hidden1(n, t):
                act.wait_ge(l1_done, tile(n, t) + 1)
                act.activation(h1[:, :, :], ps_h1[:, :, :], ACT.Relu).then_inc(h1_ready, 1)

            def hidden2(n, t):
                act.wait_ge(l2_done, tile(n, t) + 1)
                for m in range(M2):
                    act.activation(h2[:, m, :], ps_h2[:, m, :], ACT.Relu, bias=b2[:, m:m + 1]).then_inc(h2_ready, 1)

            def output(n, t):
                act.wait_ge(l3_done, tile(n, t) + 1)
                act.wait_ge(y_stored[t % 2], 16 * uses(n, t))
                act.copy(y[t % 2][0:1, :], ps_h2[0:1, M2, :]).then_inc(y_ready, 1)

            def supertile(n, first):
                act.wait_ge(dot_done[0], ST * n)
                act.wait_ge(dot_done[1], ST * n)
                for h in range(NH):
                    act.wait_ge(onehot_used[CH - 1], NH * n + h + 1)
                    act.copy(eT[:, :, :, NC + h], ps_hot[h % 2][:, :].rearrange("d (t s) -> d t s", t=ST))\
                       .then_inc(hot_read[h % 2], 1)
                for t in range(ST):
                    i = t % 2
                    for g in range(NG):
                        if tr_pair(t, g) == 0:
                            f = group(g)
                            act.wait_ge(transposed[i], NG * uses(n, t) + g + 1)
                            act.copy(eT[:, t, :, f[0]:f[-1] + 1],
                                     ps_tr[0][:, 0:len(f), :].rearrange("d f s -> d s f")).then_inc(tr_read[0], 1)
                    if not (first and t == 0):
                        hidden1(*before(n, t))
                        hidden2(*before(n, t))
                    act.wait_ge(dot_done[1], tile(n, t) + 1)
                    act.wait_ge(dots_stored[i], 64 * uses(n, t))
                    act.copy(dots[i][:, 0:NF, HG:SG], ps_dot[1][:, :, 0:NF].rearrange("p g i -> p i g"))
                    act.copy(dots[i][:, NF:IW, HG:SG], ps_dot[1][:, :, 0:NDIST].rearrange("p g i -> p i g"))\
                       .then_inc(dot_read[1], 1)
                    if not (first and t == 0):
                        output(*before(n, t))

            for h in range(1, NH, 2):
                act.dma_start(raw_tables[:, h], x["hot"][h].rearrange("(c p) d -> p c d", p=CR))\
                   .then_inc(raw_ready[h], 16)
            at = 0
            for c in range(KC):
                k = KROWS[c] - (c == 1)
                act.dma_start(w1[0:k, c, :], x["w1"][at:at + k, :]).then_inc(w1_ready, 16)
                at += k
            act.dma_start(w1[KROWS[1] - 1:KROWS[1], 1, :], x["b1"].rearrange("(a n) -> a n", a=1)).then_inc(w1_ready, 16)
            act.dma_start(w2[:, :, :], x["w2"].rearrange("(c p) n -> p c n", p=P)).then_inc(w23_ready, 16)
            with nc.allow_non_contiguous_dma(reason="256 weights onto the partitions, once"):
                act.dma_start(w3[:, :], x["w3"].rearrange("(m p) o -> p (m o)", p=P)).then_inc(w23_ready, 16)
                act.dma_start(b2[:, :], x["b2"].rearrange("(m p) -> p m", p=P)).then_inc(b2_ready, 16)
            for h in range(NH):
                act.wait_ge(raw_ready[h], 16)
                act.copy(table_hi[:, h], raw_tables[:, h]).then_inc(hi_ready, 1)
            act.wait_ge(lo_ready, NH)
            act.wait_ge(b2_ready, 16)
            supertile(0, True)
            with act.Fori(1, NS) as n:
                supertile(n, False)
            hidden1(NS - 1, ST - 1)
            hidden2(NS - 1, ST - 1)
            output(NS - 1, ST - 1)

        @block.tensor
        def _(pe):
            def lookups(n, first):
                for h in range(NH):
                    if first:
                        pe.wait_ge(lo_ready, h + 1)
                    pe.wait_ge(hot_read[h % 2], hot_uses(n, h))
                    for c in range(CH):
                        pe.wait_ge(onehot_ready, NH * CH * n + CH * h + c + 1)
                        pe.matmul(ps_hot[h % 2][:, :], table_hi[:, h, c, :], onehot[:, c, :],
                                  start=(c == 0), stop=False)
                        pe.matmul(ps_hot[h % 2][:, :], table_lo[:, h, c, :], onehot[:, c, :],
                                  start=False, stop=(c == CH - 1)).then_inc(onehot_used[c], 1)

            def transposes(n, t):
                i = t % 2
                pe.wait_ge(rows_ready[i], NC * 16 * (uses(n, t) + 1))
                for g in range(NG):
                    pair = tr_pair(t, g)
                    pe.wait_ge(tr_read[pair], bank_uses(n, t, g))
                    for f in group(g):
                        last = pe.transpose(ps_tr[pair][:, f - TG * g, :], rows[i][:, f, :], ident[:, :])
                    last.then_inc(transposed[i], 1)

            def products(n, t, q):
                if q == 0:
                    for pair in range(2):
                        pe.wait_ge(tr_read[pair], banks_through(n, t, pair))
                        pe.wait_ge(hot_read[pair], (NH // 2) * (n + 1))
                pe.wait_ge(dot_read[q], tile(n, t))
                for g in range(HG):
                    for s in range(4):
                        e = eT[:, t, SG * s + HG * q + g, :]
                        last = pe.matmul(ps_dot[q][SG * s:SG * s + NF, g, 0:NF], e, e, start=True, stop=True)
                last.then_inc(dot_done[q], 1)

            def layer1(n, t):
                i = t % 2
                pe.wait_ge(dense_ready[i], 32 * (uses(n, t) + 1))
                pe.wait_ge(z_ready[i], 16 * KC * (uses(n, t) + 1))
                pe.wait_ge(h1_ready, tile(n, t))
                for m in range(M1):
                    for c in range(KC):
                        k = KROWS[c]
                        last = pe.matmul(ps_h1[:, m, :], w1[0:k, c, m * P:(m + 1) * P], zT[i][0:k, c, :],
                                         start=(c == 0), stop=(c == KC - 1))
                last.then_inc(l1_done, 1)

            def layer2(n, t):
                pe.wait_ge(h1_ready, tile(n, t) + 1)
                pe.wait_ge(y_ready, tile(n, t))
                for m in range(M2):
                    for c in range(M1):
                        last = pe.matmul(ps_h2[:, m, :], w2[:, c, m * P:(m + 1) * P], h1[:, c, :],
                                         start=(c == 0), stop=(c == M1 - 1))
                last.then_inc(l2_done, 1)

            def layer3(n, t):
                pe.wait_ge(h2_ready, M2 * (tile(n, t) + 1))
                for m in range(M2):
                    last = pe.matmul(ps_h2[0:1, M2, :], w3[:, m:m + 1], h2[:, m, :], start=(m == 0), stop=(m == M2 - 1))
                last.then_inc(l3_done, 1)

            def supertile(n, first):
                lookups(n, first)
                for t in range(ST):
                    transposes(n, t)
                    if not (first and t == 0):
                        layer1(*before(n, t))
                    products(n, t, 0)
                    if not (first and t == 0):
                        layer2(*before(n, t))
                    products(n, t, 1)
                    if not (first and t == 0):
                        layer3(*before(n, t))

            pe.wait_ge(ident_ready, 1)
            pe.wait_ge(cleared, 4)
            pe.wait_ge(w1_ready, 16 * (KC + 1))
            pe.wait_ge(w23_ready, 32)
            supertile(0, True)
            with pe.Fori(1, NS) as n:
                supertile(n, False)
            layer1(NS - 1, ST - 1)
            layer2(NS - 1, ST - 1)
            layer3(NS - 1, ST - 1)


def kernel(**inputs):
    import numpy as np
    import concourse.bacc as bacc
    from concourse.bass_utils import run_bass_kernel_spmd

    nc = bacc.Bacc("TRN2", target_bir_lowering=False, num_devices=1)
    ids = np.ascontiguousarray(inputs["ids"])
    ids = np.concatenate([ids, ids[0:ST * P]], axis=0)
    w1 = np.ascontiguousarray(inputs["W_top1"])
    npairs = NF * NDIST
    order = pair_rows()
    w1_rows = (order[0:KP] + list(range(npairs, npairs + D0)) + order[KP:2 * KP]
               + list(range(npairs + D0, npairs + ND)) + order[2 * KP:])
    arrays = {
        "cold_ids": np.ascontiguousarray(ids[:, COLD]),
        "hot_ids": np.ascontiguousarray(ids[:, HOT].T),
        "dense": np.ascontiguousarray(np.asarray(inputs["dense_ctx"]).T),
        "w1": np.ascontiguousarray(w1[w1_rows]),
        "b1": np.ascontiguousarray(inputs["b_top1"]),
        "w2": np.ascontiguousarray(inputs["W_top2"]),
        "b2": np.ascontiguousarray(inputs["b_top2"]),
        "w3": np.ascontiguousarray(inputs["W_top3"]),
    }
    for f in range(NF):
        arrays[f"tbl_{f}"] = np.ascontiguousarray(inputs[f"tbl_{f}"])
    x = {name: nc.dram_tensor(f"in_{name}", a.shape, mybir.dt.from_np(a.dtype), kind="ExternalInput").ap()
         for name, a in arrays.items()}
    x["cold"] = [x[f"tbl_{f}"] for f in COLD]
    x["hot"] = [x[f"tbl_{f}"] for f in HOT]
    x["y"] = nc.dram_tensor("out_y", (BATCH, 1), mybir.dt.float32, kind="ExternalOutput").ap()
    dlrm_tower(nc, x)
    r = run_bass_kernel_spmd(nc, [{f"in_{name}": a for name, a in arrays.items()}], core_ids=[0])
    return r.results[0]["out_y"]
```

```python
import concourse.bass as bass
from concourse import mybir
from contextlib import ExitStack

P = 128
BATCH = 2048
NF = 27
ST = 4
NS = BATCH // (ST * P)
TABLE_ROWS = [1000, 1250, 125000, 1250, 1250, 1000, 12500, 12500, 1000, 1250, 1250, 12500, 1000, 1250, 1000, 1000,
              1250, 1000, 1250, 12500, 1250, 1000, 12500, 12500, 12500, 12500, 1250]
HOT_ROWS = 1000
HOT = [f for f in range(NF) if TABLE_ROWS[f] == HOT_ROWS]
COLD = [f for f in range(NF) if TABLE_ROWS[f] != HOT_ROWS]
SLOTS = COLD + HOT
NH, NC = len(HOT), len(COLD)
CR = 125
CH = HOT_ROWS // CR
NDIST = (NF - 1) // 2
JC = 9
KC = NF // JC
KP = JC * NDIST
ND = 16
D0 = P - KP
D1 = ND - D0
KROWS = [P, KP + D1 + 1, KP]
H1, H2 = 512, 256
M1, M2 = H1 // P, H2 // P
SG = 32
HG = SG // 2
IW = NF + NDIST
TG = 4
NG = -(-NC // TG)
NI = 4
LAG = 2


def pair_rows():
    rows = []
    for j in range(NF):
        for d in range(1, NDIST + 1):
            a, b = SLOTS[j], SLOTS[(j + d) % NF]
            hi, lo = max(a, b), min(a, b)
            rows.append(hi * (hi - 1) // 2 + lo)
    return rows


def dlrm_tower(nc, x):
    fp32, f32r, i32 = mybir.dt.float32, mybir.dt.float32r, mybir.dt.int32
    ALU = mybir.AluOpType
    ACT = mybir.ActivationFunctionType

    with ExitStack() as ctx:
        def sb(name, shape, dt=fp32):
            return ctx.enter_context(nc.sbuf_tensor(name, shape, dt))

        def ps(name, shape):
            return ctx.enter_context(nc.psum_tensor(name, shape, fp32))

        def sem(name):
            return ctx.enter_context(nc.semaphore(name))

        eT = sb("eT", [P, ST, P, NF])
        table_hi = sb("table_hi", [CR, NH, CH, P], f32r)
        table_lo = sb("table_lo", [CR, NH, CH, P], f32r)
        rows = [sb(f"rows{t}", [P, NC, P]) for t in range(ST)]
        hot_ids = [sb(f"hot_ids{i}", [P, ST * P], i32) for i in range(NI)]
        onehot = sb("onehot", [CR, CH, ST * P], f32r)
        row_number = sb("row_number", [P, CH])
        cold_ids = sb("cold_ids", [P, ST, NC], i32)
        ident = sb("ident", [P, P])
        dots = [sb(f"dots{i}", [P, IW, SG]) for i in range(2)]
        zT = [sb(f"zT{i}", [P, KC, P]) for i in range(2)]
        w1 = sb("w1", [P, KC, H1])
        w2 = sb("w2", [P, M1, H2])
        w3 = sb("w3", [P, M2])
        b2 = sb("b2", [P, M2])
        h1 = sb("h1", [P, M1, P])
        h2 = sb("h2", [P, M2, P])
        y = sb("y", [1, P])
        staging = [rows[t][0:CR, CH * k:CH * k + CH, :] for t in range(1, ST) for k in range(2)]
        staging += [dots[i][0:CR, 0:IW, :].rearrange("p i g -> p (i g)")[:, 0:CH * P]
                    .rearrange("p (c d) -> p c d", c=CH) for i in range(2)]

        scratch = [nc.dram_tensor(f"dots_scratch{i}", (SG, IW, P), fp32, kind="Internal").ap() for i in range(2)]

        ps_hot = [ps(f"ps_hot{i}", [P, ST * P]) for i in range(2)]
        ps_tr = [ps(f"ps_tr{i}", [P, TG, P]) for i in range(2)]
        ps_dot = [ps(f"ps_dot{i}", [P, HG, 32]) for i in range(2)]
        ps_h1 = ps("ps_h1", [P, M1, P])
        ps_h2 = ps("ps_h2", [P, 4, P])

        cold_ids_ready = [sem(f"cold_ids_ready{i}") for i in range(ST)]
        hot_ids_ready = [sem(f"hot_ids_ready{i}") for i in range(NI)]
        raw_ready = [sem(f"raw_ready{h}") for h in range(NH)]
        w1_ready = sem("w1_ready")
        w23_ready = sem("w23_ready")
        b2_ready = sem("b2_ready")
        dense_ready = [sem(f"dense_ready{i}") for i in range(2)]
        row_number_ready = sem("row_number_ready")
        ident_zero = sem("ident_zero")
        ident_ready = sem("ident_ready")
        cleared = sem("cleared")
        hi_ready = sem("hi_ready")
        lo_ready = sem("lo_ready")
        onehot_ready = sem("onehot_ready")
        onehot_used = [sem(f"onehot_used{i}") for i in range(CH)]
        hot_read = [sem(f"hot_read{i}") for i in range(2)]
        rows_ready = [sem(f"rows_ready{t}") for t in range(ST)]
        transposed = [sem(f"transposed{t}") for t in range(ST)]
        tr_read = [sem(f"tr_read{i}") for i in range(2)]
        dot_done = [sem(f"dot_done{i}") for i in range(2)]
        dot_read = [sem(f"dot_read{i}") for i in range(2)]
        dots_stored = [sem(f"dots_stored{i}") for i in range(2)]
        z_ready = [sem(f"z_ready{i}") for i in range(2)]
        l1_done = sem("l1_done")
        h1_ready = sem("h1_ready")
        l2_done = sem("l2_done")
        h2_ready = sem("h2_ready")
        l3_done = sem("l3_done")
        y_ready = sem("y_ready")
        y_stored = sem("y_stored")

        sync_waited = sem("sync_waited")
        pool_waited = sem("pool_waited")

        block = ctx.enter_context(nc.Block())

        def tile(n, t):
            return ST * n + t

        def uses(n, t):
            return (ST // 2) * n + t // 2

        def tr_pair(t, g):
            return (NG * t + g) % 2

        def bank_uses(n, t, g):
            return (NG * ST // 2) * n + (NG * t + g) // 2

        def banks_through(n, t, pair):
            return (NG * ST // 2) * n + (NG * (t + 1) + 1 - pair) // 2

        def hot_uses(n, h):
            return (NH // 2) * n + h // 2

        def ids_uses(n, h):
            return (NH // NI) * n + h // NI

        def behind(n, t):
            return (n, t - LAG) if t >= LAG else (n - 1, ST + t - LAG)

        LAST = [(NS - 1, t) for t in range(ST - LAG, ST)]

        def group(g):
            return range(TG * g, min(TG * g + TG, NC))

        @block.sync
        def _(sp):
            def wait(signal, count):
                sp.wait_ge(signal, count)
                sp.sem_inc(sync_waited, 1)

            def load_cold_ids(n, t):
                sp.dma_start(cold_ids[:, t, :], x["cold_ids"][bass.ds(tile(n, t) * P, P), :])\
                  .then_inc(cold_ids_ready[t], 16)

            def load_hot_ids(n, h):
                ids = x["hot_ids"][h:h + 1, bass.ds(n * (ST * P), ST * P)].rearrange("a s -> (a s)")
                sp.dma_start(hot_ids[h % NI][:, :], ids.partition_broadcast(P))\
                  .then_inc(hot_ids_ready[h % NI], 16)

            def store_y(n, t):
                wait(y_ready, tile(n, t) + 1)
                sp.dma_start(x["y"][bass.ds(tile(n, t) * P, P), :].rearrange("s o -> o s"), y[0:1, :])\
                  .then_inc(y_stored, 16)

            def supertile(n, first):
                for h in range(NI, NH):
                    wait(onehot_ready, CH * (NH * n + h - NI + 1))
                    load_hot_ids(n, h)
                for t in range(ST):
                    i = t % 2
                    samples = bass.ds(tile(n, t) * P, P)
                    if not (first and t == 0):
                        wait(l1_done, tile(n, t) - 1)
                    sp.dma_start(zT[i][KP:P, 0, :], x["dense"][0:D0, samples]).then_inc(dense_ready[i], 16)
                    sp.dma_start(zT[i][KP:KP + D1, 1, :], x["dense"][D0:ND, samples]).then_inc(dense_ready[i], 16)
                    wait(onehot_ready, CH * NH * (n + 1))
                    load_hot_ids(n + 1, t)
                    wait(rows_ready[t], NC * 16 * (n + 1))
                    load_cold_ids(n + 1, t)
                    wait(z_ready[i], 16 * KC * uses(n, t))
                    wait(dot_read[0], tile(n, t) + 1)
                    wait(dot_read[1], tile(n, t) + 1)
                    for s in range(4):
                        sp.dma_start(scratch[i][:, :, SG * s:SG * s + SG], dots[i][SG * s:SG * s + SG, :, :])\
                          .then_inc(dots_stored[i], 16)
                    wait(dots_stored[i], 64 * (uses(n, t) + 1))
                    for c in range(KC):
                        pairs = bass.AP(scratch[i].tensor, (JC * c * IW + JC * c + 1) * P,
                                        [[(IW + 1) * P, JC], [P, NDIST], [1, P]])
                        sp.dma_start(zT[i][0:KP, c, :], pairs).then_inc(z_ready[i], 16)
                    if not (first and t < LAG):
                        store_y(*behind(n, t))

            for t in range(ST):
                load_cold_ids(0, t)
            for h in range(NI):
                load_hot_ids(0, h)
            for h in range(0, NH, 2):
                sp.dma_start(staging[h], x["hot"][h].rearrange("(c p) d -> p c d", p=CR))\
                  .then_inc(raw_ready[h], 16)
            sp.wait_ge(cleared, 4)
            supertile(0, True)
            with sp.Fori(1, NS) as n:
                supertile(n, False)
            for n, t in LAST:
                store_y(n, t)
            sp.wait_ge(y_stored, 16 * ST * NS)
            for i in range(2):
                sp.wait_ge(dots_stored[i], 64 * (ST // 2) * NS)
            for t in range(ST):
                sp.wait_ge(cold_ids_ready[t], 16 * (NS + 1))
                sp.wait_ge(hot_ids_ready[t], 16 * (ids_uses(NS, t) + 1))

        @block.gpsimd
        def _(pool):
            def supertile(n, first):
                for t in range(ST):
                    if first and t:
                        pool.wait_ge(lo_ready, 2 * t)
                    pool.wait_ge(cold_ids_ready[t], 16 * (n + 1))
                    pool.wait_ge(transposed[t], NG * n)
                    pool.sem_inc(pool_waited, 1)
                    for f in range(NC):
                        pool.indirect_dma_start(
                            out=rows[t][:, f, :], out_offset=None, in_=x["cold"][f][:, :],
                            in_offset=bass.IndirectOffsetOnAxis(ap=cold_ids[:, t, f:f + 1], axis=0),
                        ).then_inc(rows_ready[t], 16)

            pool.iota(row_number[:, :], pattern=[[CR, CH]], base=0, channel_multiplier=1,
                      allow_small_or_imprecise_dtypes=True).then_inc(row_number_ready, 1)
            pool.memset(ident[:, :], 0.0).then_inc(ident_zero, 1)
            pool.wait_ge(ident_zero, 1)
            pool.affine_select(out=ident[:, :], in_=ident[:, :], compare_op=ALU.not_equal, fill=1.0, base=0,
                               pattern=[[-1, P]], channel_multiplier=1).then_inc(ident_ready, 1)
            supertile(0, True)
            with pool.Fori(1, NS) as n:
                supertile(n, False)

        @block.vector
        def _(dve):
            def split_low(h):
                dve.wait_ge(hi_ready, h + 1)
                dve.tensor_tensor(table_lo[:, h], staging[h], table_hi[:, h], ALU.subtract).then_inc(lo_ready, 1)

            def supertile(n, first):
                for h in range(NH):
                    if first:
                        split_low(h)
                    dve.wait_ge(hot_ids_ready[h % NI], 16 * (ids_uses(n, h) + 1))
                    for c in range(CH):
                        dve.wait_ge(onehot_used[c], NH * n + h)
                        dve.tensor_scalar(onehot[:, c, :], hot_ids[h % NI][0:CR, :], row_number[0:CR, c:c + 1], None,
                                          ALU.is_equal).then_inc(onehot_ready, 1)
                for t in range(ST):
                    i = t % 2
                    for g in range(NG):
                        if tr_pair(t, g) == 1:
                            f = group(g)
                            dve.wait_ge(transposed[t], NG * n + g + 1)
                            dve.wait_ge(dot_done[0], tile(n, t) - t)
                            dve.wait_ge(dot_done[1], tile(n, t) - t)
                            dve.tensor_copy(eT[:, t, :, f[0]:f[-1] + 1],
                                            ps_tr[1][:, 0:len(f), :].rearrange("d f s -> d s f"))\
                               .then_inc(tr_read[1], 1)
                    dve.wait_ge(dot_done[0], tile(n, t) + 1)
                    dve.wait_ge(dots_stored[i], 64 * uses(n, t))
                    dve.tensor_copy(dots[i][:, 0:NF, 0:HG], ps_dot[0][:, :, 0:NF].rearrange("p g i -> p i g"))
                    dve.tensor_copy(dots[i][:, NF:IW, 0:HG], ps_dot[0][:, :, 0:NDIST].rearrange("p g i -> p i g"))\
                       .then_inc(dot_read[0], 1)

            for i in range(2):
                dve.memset(zT[i][96:P, 1, :], 1.0).then_inc(cleared, 1)
            for q in range(2):
                dve.memset(ps_dot[q][:, :, :], 0.0).then_inc(cleared, 1)
            dve.wait_ge(row_number_ready, 1)
            supertile(0, True)
            with dve.Fori(1, NS) as n:
                supertile(n, False)

        @block.scalar
        def _(act):
            def hidden1(n, t):
                act.wait_ge(l1_done, tile(n, t) + 1)
                act.activation(h1[:, :, :], ps_h1[:, :, :], ACT.Relu).then_inc(h1_ready, 1)

            def hidden2(n, t):
                act.wait_ge(l2_done, tile(n, t) + 1)
                for m in range(M2):
                    act.activation(h2[:, m, :], ps_h2[:, m, :], ACT.Relu, bias=b2[:, m:m + 1]).then_inc(h2_ready, 1)

            def output(n, t):
                act.wait_ge(l3_done, tile(n, t) + 1)
                act.wait_ge(y_stored, 16 * tile(n, t))
                act.copy(y[0:1, :], ps_h2[0:1, M2, :]).then_inc(y_ready, 1)

            def supertile(n, first):
                act.wait_ge(dot_done[0], ST * n)
                act.wait_ge(dot_done[1], ST * n)
                for h in range(NH):
                    act.wait_ge(onehot_used[CH - 1], NH * n + h + 1)
                    act.copy(eT[:, :, :, NC + h], ps_hot[h % 2][:, :].rearrange("d (t s) -> d t s", t=ST))\
                       .then_inc(hot_read[h % 2], 1)
                for t in range(ST):
                    i = t % 2
                    for g in range(NG):
                        if tr_pair(t, g) == 0:
                            f = group(g)
                            act.wait_ge(transposed[t], NG * n + g + 1)
                            act.copy(eT[:, t, :, f[0]:f[-1] + 1],
                                     ps_tr[0][:, 0:len(f), :].rearrange("d f s -> d s f")).then_inc(tr_read[0], 1)
                    if not (first and t < LAG):
                        hidden1(*behind(n, t))
                        hidden2(*behind(n, t))
                    act.wait_ge(dot_done[1], tile(n, t) + 1)
                    act.wait_ge(dots_stored[i], 64 * uses(n, t))
                    act.copy(dots[i][:, 0:NF, HG:SG], ps_dot[1][:, :, 0:NF].rearrange("p g i -> p i g"))
                    act.copy(dots[i][:, NF:IW, HG:SG], ps_dot[1][:, :, 0:NDIST].rearrange("p g i -> p i g"))\
                       .then_inc(dot_read[1], 1)
                    if not (first and t < LAG):
                        output(*behind(n, t))

            for h in range(1, NH, 2):
                act.dma_start(staging[h], x["hot"][h].rearrange("(c p) d -> p c d", p=CR))\
                   .then_inc(raw_ready[h], 16)
            at = 0
            for c in range(KC):
                k = KROWS[c] - (c == 1)
                act.dma_start(w1[0:k, c, :], x["w1"][at:at + k, :]).then_inc(w1_ready, 16)
                at += k
            act.dma_start(w1[KROWS[1] - 1:KROWS[1], 1, :], x["b1"].rearrange("(a n) -> a n", a=1)).then_inc(w1_ready, 16)
            act.dma_start(w2[:, :, :], x["w2"].rearrange("(c p) n -> p c n", p=P)).then_inc(w23_ready, 16)
            with nc.allow_non_contiguous_dma(reason="256 weights onto the partitions, once"):
                act.dma_start(w3[:, :], x["w3"].rearrange("(m p) o -> p (m o)", p=P)).then_inc(w23_ready, 16)
                act.dma_start(b2[:, :], x["b2"].rearrange("(m p) -> p m", p=P)).then_inc(b2_ready, 16)
            for h in range(NH):
                act.wait_ge(raw_ready[h], 16)
                act.copy(table_hi[:, h], staging[h]).then_inc(hi_ready, 1)
            act.wait_ge(b2_ready, 16)
            supertile(0, True)
            with act.Fori(1, NS) as n:
                supertile(n, False)
            for n, t in LAST:
                hidden1(n, t)
                hidden2(n, t)
                output(n, t)

        @block.tensor
        def _(pe):
            def lookups(n, first):
                for h in range(NH):
                    if first:
                        pe.wait_ge(lo_ready, h + 1)
                    pe.wait_ge(hot_read[h % 2], hot_uses(n, h))
                    for c in range(CH):
                        pe.wait_ge(onehot_ready, NH * CH * n + CH * h + c + 1)
                        pe.matmul(ps_hot[h % 2][:, :], table_hi[:, h, c, :], onehot[:, c, :],
                                  start=(c == 0), stop=False)
                        pe.matmul(ps_hot[h % 2][:, :], table_lo[:, h, c, :], onehot[:, c, :],
                                  start=False, stop=(c == CH - 1)).then_inc(onehot_used[c], 1)

            def transposes(n, t):
                pe.wait_ge(rows_ready[t], NC * 16 * (n + 1))
                for g in range(NG):
                    pair = tr_pair(t, g)
                    pe.wait_ge(tr_read[pair], bank_uses(n, t, g))
                    for f in group(g):
                        last = pe.transpose(ps_tr[pair][:, f - TG * g, :], rows[t][:, f, :], ident[:, :])
                    last.then_inc(transposed[t], 1)

            def products(n, t, q):
                if q == 0:
                    for pair in range(2):
                        pe.wait_ge(tr_read[pair], banks_through(n, t, pair))
                        pe.wait_ge(hot_read[pair], (NH // 2) * (n + 1))
                pe.wait_ge(dot_read[q], tile(n, t))
                for g in range(HG):
                    for s in range(4):
                        e = eT[:, t, SG * s + HG * q + g, :]
                        last = pe.matmul(ps_dot[q][SG * s:SG * s + NF, g, 0:NF], e, e, start=True, stop=True)
                last.then_inc(dot_done[q], 1)

            def layer1(n, t):
                i = t % 2
                pe.wait_ge(dense_ready[i], 32 * (uses(n, t) + 1))
                pe.wait_ge(z_ready[i], 16 * KC * (uses(n, t) + 1))
                pe.wait_ge(h1_ready, tile(n, t))
                for m in range(M1):
                    for c in range(KC):
                        k = KROWS[c]
                        last = pe.matmul(ps_h1[:, m, :], w1[0:k, c, m * P:(m + 1) * P], zT[i][0:k, c, :],
                                         start=(c == 0), stop=(c == KC - 1))
                last.then_inc(l1_done, 1)

            def layer2(n, t):
                pe.wait_ge(h1_ready, tile(n, t) + 1)
                pe.wait_ge(y_ready, tile(n, t))
                for m in range(M2):
                    for c in range(M1):
                        last = pe.matmul(ps_h2[:, m, :], w2[:, c, m * P:(m + 1) * P], h1[:, c, :],
                                         start=(c == 0), stop=(c == M1 - 1))
                last.then_inc(l2_done, 1)

            def layer3(n, t):
                pe.wait_ge(h2_ready, M2 * (tile(n, t) + 1))
                for m in range(M2):
                    last = pe.matmul(ps_h2[0:1, M2, :], w3[:, m:m + 1], h2[:, m, :], start=(m == 0), stop=(m == M2 - 1))
                last.then_inc(l3_done, 1)

            def supertile(n, first):
                lookups(n, first)
                if first:
                    pe.wait_ge(w1_ready, 16 * (KC + 1))
                    pe.wait_ge(w23_ready, 32)
                for t in range(ST):
                    transposes(n, t)
                    if not (first and t < LAG):
                        layer1(*behind(n, t))
                    products(n, t, 0)
                    if not (first and t < LAG):
                        layer2(*behind(n, t))
                    products(n, t, 1)
                    if not (first and t < LAG):
                        layer3(*behind(n, t))

            pe.wait_ge(ident_ready, 1)
            pe.wait_ge(cleared, 4)
            supertile(0, True)
            with pe.Fori(1, NS) as n:
                supertile(n, False)
            for n, t in LAST:
                layer1(n, t)
                layer2(n, t)
                layer3(n, t)


def kernel(**inputs):
    import numpy as np
    import concourse.bacc as bacc
    from concourse.bass_utils import run_bass_kernel_spmd

    nc = bacc.Bacc("TRN2", target_bir_lowering=False, num_devices=1)
    ids = np.ascontiguousarray(inputs["ids"])
    ids = np.concatenate([ids, ids[0:ST * P]], axis=0)
    w1 = np.ascontiguousarray(inputs["W_top1"])
    npairs = NF * NDIST
    order = pair_rows()
    w1_rows = (order[0:KP] + list(range(npairs, npairs + D0)) + order[KP:2 * KP]
               + list(range(npairs + D0, npairs + ND)) + order[2 * KP:])
    arrays = {
        "cold_ids": np.ascontiguousarray(ids[:, COLD]),
        "hot_ids": np.ascontiguousarray(ids[:, HOT].T),
        "dense": np.ascontiguousarray(np.asarray(inputs["dense_ctx"]).T),
        "w1": np.ascontiguousarray(w1[w1_rows]),
        "b1": np.ascontiguousarray(inputs["b_top1"]),
        "w2": np.ascontiguousarray(inputs["W_top2"]),
        "b2": np.ascontiguousarray(inputs["b_top2"]),
        "w3": np.ascontiguousarray(inputs["W_top3"]),
    }
    for f in range(NF):
        arrays[f"tbl_{f}"] = np.ascontiguousarray(inputs[f"tbl_{f}"])
    x = {name: nc.dram_tensor(f"in_{name}", a.shape, mybir.dt.from_np(a.dtype), kind="ExternalInput").ap()
         for name, a in arrays.items()}
    x["cold"] = [x[f"tbl_{f}"] for f in COLD]
    x["hot"] = [x[f"tbl_{f}"] for f in HOT]
    x["y"] = nc.dram_tensor("out_y", (BATCH, 1), mybir.dt.float32, kind="ExternalOutput").ap()
    dlrm_tower(nc, x)
    r = run_bass_kernel_spmd(nc, [{f"in_{name}": a for name, a in arrays.items()}], core_ids=[0])
    return r.results[0]["out_y"]
```

```python
import concourse.bass as bass
from concourse import mybir
from contextlib import ExitStack

P = 128
BATCH = 2048
NF = 27
ST = 4
NS = BATCH // (ST * P)
TABLE_ROWS = [1000, 1250, 125000, 1250, 1250, 1000, 12500, 12500, 1000, 1250, 1250, 12500, 1000, 1250, 1000, 1000,
              1250, 1000, 1250, 12500, 1250, 1000, 12500, 12500, 12500, 12500, 1250]
HOT = [f for f in range(NF) if TABLE_ROWS[f] == 1000] + [26]
EXTRA = 20
COLD = [f for f in range(NF) if f not in HOT + [EXTRA]] + [EXTRA]
SLOTS = COLD + HOT
NH, NC = len(HOT), len(COLD)
CR = 125
CHUNKS = [TABLE_ROWS[f] // CR for f in HOT]
FROM = [sum(CHUNKS[:h]) for h in range(NH + 1)]
NCH = FROM[NH]
CH = max(CHUNKS)
EX = TABLE_ROWS[EXTRA] // CR
NU = NH + 1
SCALAR_FROM = 3
ROUNDED_BEFORE = {-1: (2,), 0: (3,), 1: (4,), 2: (5, 6), 3: (7, 8)}
NDIST = (NF - 1) // 2
JC = 9
KC = NF // JC
KP = JC * NDIST
ND = 16
D0 = P - KP
D1 = ND - D0
KROWS = [P, KP + D1 + 1, KP]
H1, H2 = 512, 256
M1, M2 = H1 // P, H2 // P
SG = 32
HG = SG // 2
IW = NF + NDIST
TG = 4
NG = -(-NC // TG)
BACK = 3
PART_ROWS = [TG * BACK, NC - TG * BACK]
FIRST_CHUNKS = EX // 2
SCALAR_CHUNKS = [FROM[h] + k for h in range(SCALAR_FROM, NH) for k in (3, 7)]
NI = 4
NO = 4
LAG1 = 2
LAG2 = 3
assert ST == 4 and LAG1 < LAG2 < ST


def pair_rows():
    rows = []
    for j in range(NF):
        for d in range(1, NDIST + 1):
            a, b = SLOTS[j], SLOTS[(j + d) % NF]
            hi, lo = max(a, b), min(a, b)
            rows.append(hi * (hi - 1) // 2 + lo)
    return rows


def dlrm_tower(nc, x):
    fp32, f32r, i32 = mybir.dt.float32, mybir.dt.float32r, mybir.dt.int32
    ALU = mybir.AluOpType
    ACT = mybir.ActivationFunctionType

    with ExitStack() as ctx:
        def sb(name, shape, dt=fp32):
            return ctx.enter_context(nc.sbuf_tensor(name, shape, dt))

        def ps(name, shape):
            return ctx.enter_context(nc.psum_tensor(name, shape, fp32))

        def sem(name):
            return ctx.enter_context(nc.semaphore(name))

        eT = sb("eT", [P, 2, P, NF + NU])
        table_hi = sb("table_hi", [CR, EX + NCH, P], f32r)
        table_lo = sb("table_lo", [CR, EX + NCH, P], f32r)
        extra_table = sb("extra_table", [CR, EX, P])
        rows = [sb(f"rows{t}", [P, NC, P]) for t in range(ST)]
        hot_ids = [sb(f"hot_ids{i}", [P, ST * P], i32) for i in range(NI)]
        onehot = sb("onehot", [CR, NO, ST * P], f32r)
        row_number = sb("row_number", [P, CH])
        cold_ids = sb("cold_ids", [P, ST, NC], i32)
        ident = sb("ident", [P, P])
        dots = [sb(f"dots{i}", [P, IW, SG]) for i in range(2)]
        zT = [sb(f"zT{i}", [P, KC, P]) for i in range(2)]
        w1 = sb("w1", [P, KC, H1])
        w2 = sb("w2", [P, M1, H2])
        w3 = sb("w3", [P, M2])
        b2 = sb("b2", [P, M2])
        h1 = sb("h1", [P, M1, P])
        h2 = sb("h2", [P, M2, P])
        y = sb("y", [1, P])
        distance = h1[0:CR, :, :].rearrange("p m s -> p (m s)")
        staging = [w2[0:CR, :, :].rearrange("p c n -> p (c n)")]
        staging += [rows[t][0:CR, 8 * k:8 * k + 8, :].rearrange("p c d -> p (c d)")
                    for t in range(1, ST) for k in range(2)]
        staging += [dots[i][0:CR, :, :].rearrange("p i g -> p (i g)") for i in (1, 0)]
        staging = [staging[h][:, 0:CHUNKS[h] * P].rearrange("p (c d) -> p c d", d=P) for h in range(NH)]

        scratch = [nc.dram_tensor(f"dots_scratch{i}", (NF, IW, P), fp32, kind="Internal").ap() for i in range(2)]

        ps_hot = [ps(f"ps_hot{i}", [P, ST * P]) for i in range(2)]
        ps_tr = [ps(f"ps_tr{i}", [P, TG, P]) for i in range(2)]
        ps_dot = [ps(f"ps_dot{i}", [P, HG, 32]) for i in range(2)]
        ps_h1 = ps("ps_h1", [P, M1, P])
        ps_h2 = ps("ps_h2", [P, 4, P])

        last_h1 = [ps_hot[0][:, 0:P], ps_hot[1][:, 0:P], ps_tr[0][:, 0, :], ps_tr[1][:, 0, :]]
        last_h2 = [ps_dot[0][:, 0:P // 32, :].rearrange("p g i -> p (g i)"), ps_h1[:, 0, :]]

        cold_ids_ready = [sem(f"cold_ids_ready{i}") for i in range(ST)]
        hot_ids_ready = [sem(f"hot_ids_ready{i}") for i in range(NI)]
        raw_ready = [sem(f"raw_ready{h}") for h in range(NH)]
        extra_ready = [sem(f"extra_ready{half}") for half in range(2)]
        hi_half_ready = sem("hi_half_ready")
        w1_ready = sem("w1_ready")
        w2_ready = sem("w2_ready")
        w3_ready = sem("w3_ready")
        b2_ready = sem("b2_ready")
        dense_ready = [sem(f"dense_ready{i}") for i in range(2)]
        row_number_ready = sem("row_number_ready")
        ident_zero = sem("ident_zero")
        ident_ready = sem("ident_ready")
        cleared = sem("cleared")
        hi_ready = sem("hi_ready")
        lo_ready = sem("lo_ready")
        onehot_ready = sem("onehot_ready")
        distance_ready = sem("distance_ready")
        scalar_onehot_ready = sem("scalar_onehot_ready")
        onehot_used = sem("onehot_used")
        hot_read = [sem(f"hot_read{i}") for i in range(2)]
        rows_ready = [[sem(f"rows_ready{t}_{part}") for part in range(2)] for t in range(ST)]
        transposed = [sem(f"transposed{t}") for t in range(ST)]
        tr_read = [sem(f"tr_read{i}") for i in range(2)]
        dot_done = [sem(f"dot_done{i}") for i in range(2)]
        dot_read = [sem(f"dot_read{i}") for i in range(2)]
        dots_stored = [sem(f"dots_stored{i}") for i in range(2)]
        z_ready = [sem(f"z_ready{i}") for i in range(2)]
        l1_done = sem("l1_done")
        h1_ready = sem("h1_ready")
        l2_done = sem("l2_done")
        h2_ready = sem("h2_ready")
        l3_done = sem("l3_done")
        l1_part_done = sem("l1_part_done")
        h1_part_ready = sem("h1_part_ready")
        l2_part_done = sem("l2_part_done")
        h2_part_ready = sem("h2_part_ready")
        y_ready = sem("y_ready")
        y_stored = sem("y_stored")

        sync_waited = sem("sync_waited")
        pool_waited = sem("pool_waited")

        block = ctx.enter_context(nc.Block())

        def tile(n, t):
            return ST * n + t

        def uses(n, t):
            return (ST // 2) * n + t // 2

        def column0(t):
            return NU * (t // 2)

        def gathered(first):
            return NC - 1 if first else NC

        def landed(n, part):
            return 16 * (PART_ROWS[part] * (n + 1) - (part == 1))

        def tr_pair(t, g):
            return (NG * t + g) % 2

        def bank_uses(n, t, g):
            return (NG * ST // 2) * n + (NG * t + g) // 2

        def banks_through(n, t, pair):
            return (NG * ST // 2) * n + (NG * (t + 1) + 1 - pair) // 2

        def hot_uses(n, h):
            return len(range(h % 2, NH, 2)) * n + h // 2 + h % 2

        def ids_uses(n, h):
            return len(range(h % NI, NH, NI)) * n + h // NI + (h % NI == NI - 1)

        def slot_before(n, c):
            if c >= NO or (isinstance(n, int) and n == 0):
                return EX + NCH * n + c - NO + 1
            return EX + NCH * (n - 1) + max(range(c % NO, NCH, NO)) + 1

        def chunks(h):
            return range(FROM[h], FROM[h + 1]) if h >= 0 else range(-EX, 0)

        def tables(first):
            return range(-1 if first else 0, NH)

        def in_table(table, h):
            return table[:, EX + chunks(h)[0]:EX + chunks(h)[-1] + 1]

        def behind(n, t, lag):
            return (n, t - lag) if t >= lag else (n - 1, ST + t - lag)

        LAST = [(NS - 1, t) for t in range(ST)]

        def group(g, first):
            return range(TG * g, min(TG * g + TG, gathered(first)))

        def vector_chunks(n, first, c):
            return EX + NCH * n + c - (scalar_chunks(c) if first else 0)

        def scalar_chunks(c):
            return len([k for k in SCALAR_CHUNKS if k < c])

        def load_table(engine, h):
            engine.dma_start(staging[h], x["hot"][h].rearrange("(c p) d -> p c d", p=CR)).then_inc(raw_ready[h], 16)

        @block.sync
        def _(sp):
            def wait(signal, count):
                sp.wait_ge(signal, count)
                sp.sem_inc(sync_waited, 1)

            def load_cold_ids(n, t):
                sp.dma_start(cold_ids[:, t, :], x["cold_ids"][bass.ds(tile(n, t) * P, P), :])\
                  .then_inc(cold_ids_ready[t], 16)

            def load_hot_ids(n, h):
                row = h % (NH + 1)
                ids = x["hot_ids"][row:row + 1, bass.ds(n * (ST * P), ST * P)].rearrange("a s -> (a s)")
                sp.dma_start(hot_ids[h % NI][:, :], ids.partition_broadcast(P))\
                  .then_inc(hot_ids_ready[h % NI], 16)

            def store_y(n, t):
                wait(y_ready, tile(n, t) + 1)
                sp.dma_start(x["y"][bass.ds(tile(n, t) * P, P), :].rearrange("s o -> o s"), y[0:1, :])\
                  .then_inc(y_stored, 16)

            def load_weights():
                at = 0
                for c in range(KC):
                    k = KROWS[c] - (c == 1)
                    sp.dma_start(w1[0:k, c, :], x["w1"][at:at + k, :]).then_inc(w1_ready, 16)
                    at += k
                bias_row = w1[KROWS[1] - 1:KROWS[1], 1, :]
                sp.dma_start(bias_row, x["b1"].rearrange("(a n) -> a n", a=1)).then_inc(w1_ready, 16)
                with nc.allow_non_contiguous_dma(reason="256 weights onto the partitions, once"):
                    sp.dma_start(w3[:, :], x["w3"].rearrange("(m p) o -> p (m o)", p=P)).then_inc(w3_ready, 16)
                    sp.dma_start(b2[:, :], x["b2"].rearrange("(m p) -> p m", p=P)).then_inc(b2_ready, 16)
                sp.wait_ge(lo_ready, 3)
                sp.dma_start(w2[:, :, :], x["w2"].rearrange("(c p) n -> p c n", p=P)).then_inc(w2_ready, 16)
                sp.wait_ge(cleared, 4)

            def supertile(n, first=False, final=False):
                for h in range(NI - 1 if first else NI, NH):
                    wait(onehot_ready, vector_chunks(n, first, FROM[h - NI + 1]))
                    if first and h - NI >= SCALAR_FROM:
                        sp.wait_ge(scalar_onehot_ready, scalar_chunks(FROM[h - NI + 1]))
                    load_hot_ids(n, h)
                if first:
                    load_weights()
                if not final:
                    wait(onehot_ready, EX + NCH * (n + 1))
                for t in range(ST):
                    i = t % 2
                    samples = bass.ds(tile(n, t) * P, P)
                    wait(z_ready[i], 16 * KC * uses(n, t))
                    wait(dot_read[0], tile(n, t) + 1)
                    wait(dot_read[1], tile(n, t) + 1)
                    for s in range(4):
                        sp.dma_start(scratch[i][:, :, SG * s:SG * s + SG], dots[i][SG * s:SG * s + NF, :, :])\
                          .then_inc(dots_stored[i], 16)
                    if not (first and t == 0):
                        wait(l1_done, tile(n, t) - 1)
                    sp.dma_start(zT[i][KP:P, 0, :], x["dense"][0:D0, samples]).then_inc(dense_ready[i], 16)
                    sp.dma_start(zT[i][KP:KP + D1, 1, :], x["dense"][D0:ND, samples]).then_inc(dense_ready[i], 16)
                    if not (first and t < LAG2):
                        store_y(*behind(n, t, LAG2))
                    if not final:
                        load_hot_ids(n + 1, t)
                        for part in range(2):
                            wait(rows_ready[t][part], landed(n, part))
                        load_cold_ids(n + 1, t)
                    wait(dots_stored[i], 64 * (uses(n, t) + 1))
                    for c in range(KC):
                        pairs = bass.AP(scratch[i].tensor, (JC * c * IW + JC * c + 1) * P,
                                        [[(IW + 1) * P, JC], [P, NDIST], [1, P]])
                        sp.dma_start(zT[i][0:KP, c, :], pairs).then_inc(z_ready[i], 16)

            load_cold_ids(0, 0)
            for i in range(NI):
                load_hot_ids(0, i - 1)
                load_table(sp, 2 * i)
            load_table(sp, NH - 1)
            for t in range(1, ST):
                load_cold_ids(0, t)
            supertile(0, first=True)
            with sp.Fori(1, NS - 1) as n:
                supertile(n)
            supertile(NS - 1, final=True)
            for n, t in LAST[ST - LAG2:]:
                store_y(n, t)
            sp.wait_ge(y_stored, 16 * ST * NS)
            for i in range(2):
                sp.wait_ge(dots_stored[i], 64 * (ST // 2) * NS)

        @block.gpsimd
        def _(pool):
            def supertile(n, first=False):
                for t in range(ST):
                    if first and t:
                        pool.wait_ge(lo_ready, 2 * t + 3)
                    pool.wait_ge(cold_ids_ready[t], 16 * (n + 1))
                    pool.wait_ge(transposed[t], NG * n)
                    pool.sem_inc(pool_waited, 1)
                    for f in range(gathered(first)):
                        pool.indirect_dma_start(
                            out=rows[t][:, f, :], out_offset=None, in_=x["cold"][f][:, :],
                            in_offset=bass.IndirectOffsetOnAxis(ap=cold_ids[:, t, f:f + 1], axis=0),
                        ).then_inc(rows_ready[t][f // (TG * BACK)], 16)

            pool.iota(row_number[:, :], pattern=[[CR, CH]], base=0, channel_multiplier=1,
                      allow_small_or_imprecise_dtypes=True).then_inc(row_number_ready, 1)
            pool.memset(ident[:, :], 0.0).then_inc(ident_zero, 1)
            pool.wait_ge(ident_zero, 1)
            pool.affine_select(out=ident[:, :], in_=ident[:, :], compare_op=ALU.not_equal, fill=1.0, base=0,
                               pattern=[[-1, P]], channel_multiplier=1).then_inc(ident_ready, 1)
            supertile(0, first=True)
            with pool.Fori(1, NS) as n:
                supertile(n)

        @block.vector
        def _(dve):
            def split_half(half):
                local = slice(half * FIRST_CHUNKS, (half + 1) * FIRST_CHUNKS)
                dve.wait_ge(extra_ready[half], 16)
                dve.tensor_copy(table_hi[:, local], extra_table[:, local]).then_inc(hi_half_ready, 1)
                dve.wait_ge(hi_half_ready, half + 1)
                dve.tensor_tensor(table_lo[:, local], extra_table[:, local], table_hi[:, local],
                                  ALU.subtract).then_inc(lo_ready, 1)

            def split_low(h):
                dve.wait_ge(hi_ready, h + 1)
                dve.tensor_tensor(in_table(table_lo, h), staging[h], in_table(table_hi, h), ALU.subtract)\
                   .then_inc(lo_ready, 1)

            def supertile(n, first=False):
                for h in tables(first):
                    if first and h >= 0:
                        split_low(h)
                    for c in chunks(h):
                        if h == -1 and (c + EX) % FIRST_CHUNKS == 0:
                            split_half((c + EX) // FIRST_CHUNKS)
                        if c == chunks(h)[0]:
                            dve.wait_ge(hot_ids_ready[h % NI], 16 * (ids_uses(n, h) + 1))
                        if first and c in SCALAR_CHUNKS:
                            continue
                        if not (first and c < NO - EX):
                            dve.wait_ge(onehot_used, slot_before(n, c))
                        k = c - chunks(h)[0]
                        row = row_number[0:CR, k:k + 1]
                        dve.tensor_scalar(onehot[:, c % NO, :], hot_ids[h % NI][0:CR, :], row, None,
                                          ALU.is_equal).then_inc(onehot_ready, 1)
                if first:
                    dve.wait_ge(onehot_used, EX + NCH)
                    dve.wait_ge(scalar_onehot_ready, len(SCALAR_CHUNKS))
                    dve.sem_inc(onehot_ready, len(SCALAR_CHUNKS))
                for t in range(ST):
                    i = t % 2
                    for g in range(NG):
                        if tr_pair(t, g) == 1:
                            f = group(g, first)
                            dve.wait_ge(transposed[t], NG * n + g + 1)
                            if not (first and t == 0):
                                dve.wait_ge(dot_done[0], tile(n, t) - 1)
                                dve.wait_ge(dot_done[1], tile(n, t) - 1)
                            at = column0(t) + f[0]
                            dve.tensor_copy(eT[:, i, :, at:at + len(f)],
                                            ps_tr[1][:, 0:len(f), :].rearrange("d f s -> d s f"))\
                               .then_inc(tr_read[1], 1)
                    dve.wait_ge(dot_done[0], tile(n, t) + 1)
                    dve.wait_ge(dots_stored[i], 64 * uses(n, t))
                    dve.tensor_copy(dots[i][:, 0:NF, 0:HG], ps_dot[0][:, :, 0:NF].rearrange("p g i -> p i g"))
                    dve.tensor_copy(dots[i][:, NF:IW, 0:HG], ps_dot[0][:, :, 0:NDIST].rearrange("p g i -> p i g"))\
                       .then_inc(dot_read[0], 1)

            for i in range(2):
                dve.memset(zT[i][96:P, 1, :], 1.0).then_inc(cleared, 1)
            for q in range(2):
                dve.memset(ps_dot[q][:, :, :], 0.0).then_inc(cleared, 1)
            dve.wait_ge(row_number_ready, 1)
            supertile(0, first=True)
            with dve.Fori(1, NS) as n:
                supertile(n)

        @block.scalar
        def _(act):
            def split_high(h):
                act.wait_ge(raw_ready[h], 16)
                act.copy(in_table(table_hi, h), staging[h]).then_inc(hi_ready, 1)

            def one_hot(h, c):
                act.wait_ge(hot_ids_ready[h % NI], 16 * (ids_uses(0, h) + 1))
                if scalar_chunks(c):
                    act.wait_ge(scalar_onehot_ready, scalar_chunks(c))
                act.activation(distance, hot_ids[h % NI][0:CR, :], ACT.Abs, scale=-1.0,
                               bias=row_number[0:CR, c - FROM[h]:c - FROM[h] + 1]).then_inc(distance_ready, 1)
                act.wait_ge(distance_ready, scalar_chunks(c + 1))
                act.wait_ge(onehot_used, slot_before(0, c))
                act.activation(onehot[:, c % NO, :], distance, ACT.Relu, scale=-1.0, bias=1.0)\
                   .then_inc(scalar_onehot_ready, 1)

            def hidden1(n, t):
                act.wait_ge(l1_done, tile(n, t) + 1)
                act.activation(h1[:, :, :], ps_h1[:, :, :], ACT.Relu).then_inc(h1_ready, 1)

            def hidden2(n, t):
                act.wait_ge(l2_done, tile(n, t) + 1)
                for m in range(M2):
                    act.activation(h2[:, m, :], ps_h2[:, m, :], ACT.Relu, bias=b2[:, m:m + 1]).then_inc(h2_ready, 1)

            def output(n, t):
                act.wait_ge(l3_done, tile(n, t) + 1)
                act.wait_ge(y_stored, 16 * tile(n, t))
                act.copy(y[0:1, :], ps_h2[0:1, M2, :]).then_inc(y_ready, 1)

            def products_out(n, t):
                i = t % 2
                act.wait_ge(dot_done[1], tile(n, t) + 1)
                act.wait_ge(dots_stored[i], 64 * uses(n, t))
                act.copy(dots[i][:, 0:NF, HG:SG], ps_dot[1][:, :, 0:NF].rearrange("p g i -> p i g"))
                act.copy(dots[i][:, NF:IW, HG:SG], ps_dot[1][:, :, 0:NDIST].rearrange("p g i -> p i g"))\
                   .then_inc(dot_read[1], 1)

            def supertile(n, first=False):
                act.wait_ge(dot_done[0], ST * n)
                act.wait_ge(dot_done[1], ST * n)
                for h in tables(first):
                    for table in ROUNDED_BEFORE.get(h, ()) if first else ():
                        split_high(table)
                    own = [c for c in SCALAR_CHUNKS if first and h + 1 < NH and FROM[h + 1] <= c < FROM[h + 2]]
                    for c in own[:1]:
                        one_hot(h + 1, c)
                    act.wait_ge(onehot_used, EX + NCH * n + chunks(h)[-1] + 1)
                    act.copy(eT[:, :, :, NC + h:NC + h + NU + 1:NU],
                             ps_hot[h % 2][:, :].rearrange("d (a b s) -> d b s a", a=2, b=2))\
                       .then_inc(hot_read[h % 2], 1)
                    for c in own[1:]:
                        one_hot(h + 1, c)
                for t in range(ST):
                    for g in range(NG):
                        if tr_pair(t, g) == 0:
                            f = group(g, first)
                            act.wait_ge(transposed[t], NG * n + g + 1)
                            if not (first and t == 0):
                                act.wait_ge(dot_done[0], tile(n, t) - 1)
                                act.wait_ge(dot_done[1], tile(n, t) - 1)
                            at = column0(t) + f[0]
                            act.copy(eT[:, t % 2, :, at:at + len(f)],
                                     ps_tr[0][:, 0:len(f), :].rearrange("d f s -> d s f")).then_inc(tr_read[0], 1)
                    if first and t == LAG2:
                        act.wait_ge(b2_ready, 16)
                    if not (first and t < LAG2):
                        hidden2(*behind(n, t, LAG2))
                    if not (first and t < LAG1):
                        hidden1(*behind(n, t, LAG1))
                    if not (first and t < LAG2):
                        output(*behind(n, t, LAG2))
                    products_out(n, t)

            raw = x["extra"].rearrange("(c p) d -> p c d", p=CR)
            for half in range(2):
                local = slice(half * FIRST_CHUNKS, (half + 1) * FIRST_CHUNKS)
                act.dma_start(extra_table[:, local], raw[:, local]).then_inc(extra_ready[half], 16)
            for h in range(1, NH, 2):
                load_table(act, h)
            for h in (0, 1):
                split_high(h)
            act.wait_ge(row_number_ready, 1)
            supertile(0, first=True)
            with act.Fori(1, NS) as n:
                supertile(n)
            hidden2(*LAST[1])
            hidden1(*LAST[2])
            output(*LAST[1])
            hidden2(*LAST[2])
            for m in range(M1):
                act.wait_ge(l1_part_done, m + 1)
                act.activation(h1[:, m, :], last_h1[m], ACT.Relu).then_inc(h1_part_ready, 1)
            output(*LAST[2])
            for m in range(M2):
                act.wait_ge(l2_part_done, m + 1)
                act.activation(h2[:, m, :], last_h2[m], ACT.Relu, bias=b2[:, m:m + 1]).then_inc(h2_part_ready, 1)
            output(*LAST[3])

        @block.tensor
        def _(pe):
            def lookups(n, first):
                for h in tables(first):
                    if first:
                        pe.wait_ge(lo_ready, h + 3 if h >= 0 else 1)
                    pe.wait_ge(hot_read[h % 2], hot_uses(n, h))
                    for c in chunks(h):
                        if c == FIRST_CHUNKS - EX:
                            pe.wait_ge(lo_ready, 2)
                        if first and c in SCALAR_CHUNKS:
                            pe.wait_ge(scalar_onehot_ready, scalar_chunks(c + 1))
                        else:
                            pe.wait_ge(onehot_ready, vector_chunks(n, first, c + 1))
                        pe.matmul(ps_hot[h % 2][:, :], table_hi[:, EX + c, :], onehot[:, c % NO, :],
                                  start=(c == chunks(h)[0]), stop=False)
                        pe.matmul(ps_hot[h % 2][:, :], table_lo[:, EX + c, :], onehot[:, c % NO, :],
                                  start=False, stop=(c == chunks(h)[-1])).then_inc(onehot_used, 1)

            def transposes(n, t, g, first):
                if g in (0, BACK):
                    part = g // BACK
                    pe.wait_ge(rows_ready[t][part], landed(n, part))
                pair = tr_pair(t, g)
                pe.wait_ge(tr_read[pair], bank_uses(n, t, g))
                for f in group(g, first):
                    last = pe.transpose(ps_tr[pair][:, f - TG * g, :], rows[t][:, f, :], ident[:, :])
                last.then_inc(transposed[t], 1)

            def products(n, t, q):
                if q == 0:
                    for pair in range(2):
                        pe.wait_ge(tr_read[pair], banks_through(n, t, pair))
                        pe.wait_ge(hot_read[pair], hot_uses(n + 1, pair))
                pe.wait_ge(dot_read[q], tile(n, t))
                for g in range(HG):
                    for s in range(4):
                        e = eT[:, t % 2, SG * s + HG * q + g, column0(t):column0(t) + NF]
                        last = pe.matmul(ps_dot[q][SG * s:SG * s + NF, g, 0:NF], e, e, start=True, stop=True)
                last.then_inc(dot_done[q], 1)

            def layer1(n, t, m, parts=False):
                i = t % 2
                if m == 0:
                    pe.wait_ge(dense_ready[i], 32 * (uses(n, t) + 1))
                    pe.wait_ge(z_ready[i], 16 * KC * (uses(n, t) + 1))
                    pe.wait_ge(h1_ready, tile(n, t))
                out = last_h1[m] if parts else ps_h1[:, m, :]
                for c in range(KC):
                    k = KROWS[c]
                    last = pe.matmul(out, w1[0:k, c, m * P:(m + 1) * P], zT[i][0:k, c, :],
                                     start=(c == 0), stop=(c == KC - 1))
                if parts:
                    last.then_inc(l1_part_done, 1)
                elif m == M1 - 1:
                    last.then_inc(l1_done, 1)

            def layer2(n, t, parts=False):
                if not parts:
                    pe.wait_ge(h1_ready, tile(n, t) + 1)
                    pe.wait_ge(y_ready, tile(n, t))
                else:
                    pe.wait_ge(dot_read[0], NS * ST)
                for m in range(M2):
                    out = last_h2[m] if parts else ps_h2[:, m, :]
                    for c in range(M1):
                        if parts and m == 0:
                            pe.wait_ge(h1_part_ready, c + 1)
                        last = pe.matmul(out, w2[:, c, m * P:(m + 1) * P], h1[:, c, :],
                                         start=(c == 0), stop=(c == M1 - 1))
                    if parts:
                        last.then_inc(l2_part_done, 1)
                if not parts:
                    last.then_inc(l2_done, 1)

            def layer3(n, t, parts=False):
                if not parts:
                    pe.wait_ge(h2_ready, M2 * (tile(n, t) + 1))
                else:
                    pe.wait_ge(y_ready, tile(n, t))
                for m in range(M2):
                    if parts:
                        pe.wait_ge(h2_part_ready, m + 1)
                    last = pe.matmul(ps_h2[0:1, M2, :], w3[:, m:m + 1], h2[:, m, :], start=(m == 0), stop=(m == M2 - 1))
                last.then_inc(l3_done, 1)

            def supertile(n, first=False):
                lookups(n, first)
                if first:
                    pe.wait_ge(w1_ready, 16 * (KC + 1))
                    pe.wait_ge(w2_ready, 16)
                    pe.wait_ge(w3_ready, 16)
                for t in range(ST):
                    for g in range(NG):
                        if g and not (first and t <= LAG1):
                            layer1(*behind(n, t, LAG1), g - 1)
                        transposes(n, t, g, first)
                    if not (first and t < LAG2):
                        layer2(*behind(n, t, LAG2))
                    products(n, t, 0)
                    if first and t == LAG1:
                        for m in range(M1):
                            layer1(n, 0, m)
                    if not (first and t < LAG2):
                        layer3(*behind(n, t, LAG2))
                    products(n, t, 1)

            pe.wait_ge(ident_ready, 1)
            pe.wait_ge(cleared, 4)
            supertile(0, first=True)
            with pe.Fori(1, NS) as n:
                supertile(n)
            layer2(*LAST[1])
            for m in range(M1):
                layer1(*LAST[2], m)
            layer3(*LAST[1])
            layer2(*LAST[2])
            for m in range(M1):
                layer1(*LAST[3], m, parts=True)
            layer3(*LAST[2])
            layer2(*LAST[3], parts=True)
            layer3(*LAST[3], parts=True)


def kernel(**inputs):
    import numpy as np
    import concourse.bacc as bacc
    from concourse.bass_utils import run_bass_kernel_spmd

    nc = bacc.Bacc("TRN2", target_bir_lowering=False, num_devices=1)
    ids = np.ascontiguousarray(inputs["ids"])
    w1 = np.ascontiguousarray(inputs["W_top1"])
    npairs = NF * NDIST
    order = pair_rows()
    w1_rows = (order[0:KP] + list(range(npairs, npairs + D0)) + order[KP:2 * KP]
               + list(range(npairs + D0, npairs + ND)) + order[2 * KP:])
    arrays = {
        "cold_ids": np.ascontiguousarray(ids[:, COLD]),
        "hot_ids": np.ascontiguousarray(ids[:, HOT + [EXTRA]].T),
        "dense": np.ascontiguousarray(np.asarray(inputs["dense_ctx"]).T),
        "w1": np.ascontiguousarray(w1[w1_rows]),
        "b1": np.ascontiguousarray(inputs["b_top1"]),
        "w2": np.ascontiguousarray(inputs["W_top2"]),
        "b2": np.ascontiguousarray(inputs["b_top2"]),
        "w3": np.ascontiguousarray(inputs["W_top3"]),
    }
    for f in range(NF):
        arrays[f"tbl_{f}"] = np.ascontiguousarray(inputs[f"tbl_{f}"])
    x = {name: nc.dram_tensor(f"in_{name}", a.shape, mybir.dt.from_np(a.dtype), kind="ExternalInput").ap()
         for name, a in arrays.items()}
    x["cold"] = [x[f"tbl_{f}"] for f in COLD]
    x["extra"] = x[f"tbl_{EXTRA}"]
    x["hot"] = [x[f"tbl_{f}"] for f in HOT]
    x["y"] = nc.dram_tensor("out_y", (BATCH, 1), mybir.dt.float32, kind="ExternalOutput").ap()
    dlrm_tower(nc, x)
    r = run_bass_kernel_spmd(nc, [{f"in_{name}": a for name, a in arrays.items()}], core_ids=[0])
    return r.results[0]["out_y"]
```
